# Optimizing a Trainium2 kernel written in Bass

```python
import numpy as np
import jax
import jax.numpy as jnp

def _softmax(x, axis=-1):
    return jax.nn.softmax(x, axis=axis)

def _gelu(x):
    return jax.nn.gelu(x, approximate=True)

def _silu(x):
    return jax.nn.silu(x)

def _sigmoid(x):
    return jax.nn.sigmoid(x)

def _layernorm(x, axis=-1, eps=1e-05):
    m = jnp.mean(x, axis=axis, keepdims=True)
    v = jnp.var(x, axis=axis, keepdims=True)
    return (x - m) / jnp.sqrt(v + eps)

def _scatter_add(tgt, idx, src, axis=0):
    return tgt.at[idx].add(src)

def _segment_sum(src, seg, n):
    return jax.ops.segment_sum(src, seg, n)
kernel_name = 'mk_dlrm_tower_d1_rec_r8_6b6c65'

def setup_inputs(seed: int=0):
    np.random.seed(seed)
    _w = jnp.asarray

    def _rec_inputs():
        import jax
        import jax.numpy as jnp
        _tk = jax.random.key(seed)
        dense_ctx = jax.random.normal(jax.random.fold_in(_tk, 190), (512, 16), jnp.float32)
        ids = jnp.stack([jax.random.randint(jax.random.fold_in(_tk, 200 + f), (512,), 0, v, jnp.int32) for f, v in enumerate([12500, 12500, 12500, 125000, 1250, 12500, 12500, 1000, 12500, 1250, 1000, 12500, 12500, 1000, 1000, 1250, 1250, 12500, 1000, 1000, 1000, 1000, 1000, 1000, 1000, 1000, 1000])], axis=1)
        tbl_0 = 0.05 * jax.random.normal(jax.random.fold_in(_tk, 500 + 0), (12500, 128), jnp.float32)
        tbl_1 = 0.05 * jax.random.normal(jax.random.fold_in(_tk, 500 + 1), (12500, 128), jnp.float32)
        tbl_2 = 0.05 * jax.random.normal(jax.random.fold_in(_tk, 500 + 2), (12500, 128), jnp.float32)
        tbl_3 = 0.05 * jax.random.normal(jax.random.fold_in(_tk, 500 + 3), (125000, 128), jnp.float32)
        tbl_4 = 0.05 * jax.random.normal(jax.random.fold_in(_tk, 500 + 4), (1250, 128), jnp.float32)
        tbl_5 = 0.05 * jax.random.normal(jax.random.fold_in(_tk, 500 + 5), (12500, 128), jnp.float32)
        tbl_6 = 0.05 * jax.random.normal(jax.random.fold_in(_tk, 500 + 6), (12500, 128), jnp.float32)
        tbl_7 = 0.05 * jax.random.normal(jax.random.fold_in(_tk, 500 + 7), (1000, 128), jnp.float32)
        tbl_8 = 0.05 * jax.random.normal(jax.random.fold_in(_tk, 500 + 8), (12500, 128), jnp.float32)
        tbl_9 = 0.05 * jax.random.normal(jax.random.fold_in(_tk, 500 + 9), (1250, 128), jnp.float32)
        tbl_10 = 0.05 * jax.random.normal(jax.random.fold_in(_tk, 500 + 10), (1000, 128), jnp.float32)
        tbl_11 = 0.05 * jax.random.normal(jax.random.fold_in(_tk, 500 + 11), (12500, 128), jnp.float32)
        tbl_12 = 0.05 * jax.random.normal(jax.random.fold_in(_tk, 500 + 12), (12500, 128), jnp.float32)
        tbl_13 = 0.05 * jax.random.normal(jax.random.fold_in(_tk, 500 + 13), (1000, 128), jnp.float32)
        tbl_14 = 0.05 * jax.random.normal(jax.random.fold_in(_tk, 500 + 14), (1000, 128), jnp.float32)
        tbl_15 = 0.05 * jax.random.normal(jax.random.fold_in(_tk, 500 + 15), (1250, 128), jnp.float32)
        tbl_16 = 0.05 * jax.random.normal(jax.random.fold_in(_tk, 500 + 16), (1250, 128), jnp.float32)
        tbl_17 = 0.05 * jax.random.normal(jax.random.fold_in(_tk, 500 + 17), (12500, 128), jnp.float32)
        tbl_18 = 0.05 * jax.random.normal(jax.random.fold_in(_tk, 500 + 18), (1000, 128), jnp.float32)
        tbl_19 = 0.05 * jax.random.normal(jax.random.fold_in(_tk, 500 + 19), (1000, 128), jnp.float32)
        tbl_20 = 0.05 * jax.random.normal(jax.random.fold_in(_tk, 500 + 20), (1000, 128), jnp.float32)
        tbl_21 = 0.05 * jax.random.normal(jax.random.fold_in(_tk, 500 + 21), (1000, 128), jnp.float32)
        tbl_22 = 0.05 * jax.random.normal(jax.random.fold_in(_tk, 500 + 22), (1000, 128), jnp.float32)
        tbl_23 = 0.05 * jax.random.normal(jax.random.fold_in(_tk, 500 + 23), (1000, 128), jnp.float32)
        tbl_24 = 0.05 * jax.random.normal(jax.random.fold_in(_tk, 500 + 24), (1000, 128), jnp.float32)
        tbl_25 = 0.05 * jax.random.normal(jax.random.fold_in(_tk, 500 + 25), (1000, 128), jnp.float32)
        tbl_26 = 0.05 * jax.random.normal(jax.random.fold_in(_tk, 500 + 26), (1000, 128), jnp.float32)
        _rk = jax.random.fold_in(_tk, 7)
        W_top1 = 0.0521996 * jax.random.normal(jax.random.fold_in(_tk, 801), (367, 512), jnp.float32)
        W_top2 = 0.0441942 * jax.random.normal(jax.random.fold_in(_tk, 802), (512, 256), jnp.float32)
        W_top3 = 0.0625 * jax.random.normal(jax.random.fold_in(_tk, 803), (256, 1), jnp.float32)
        b_top1 = jnp.zeros((512,), jnp.float32)
        b_top2 = jnp.zeros((256,), jnp.float32)
        return (dense_ctx, ids, tbl_0, tbl_1, tbl_2, tbl_3, tbl_4, tbl_5, tbl_6, tbl_7, tbl_8, tbl_9, tbl_10, tbl_11, tbl_12, tbl_13, tbl_14, tbl_15, tbl_16, tbl_17, tbl_18, tbl_19, tbl_20, tbl_21, tbl_22, tbl_23, tbl_24, tbl_25, tbl_26, W_top1, b_top1, W_top2, b_top2, W_top3)
    dense_ctx, ids, tbl_0, tbl_1, tbl_2, tbl_3, tbl_4, tbl_5, tbl_6, tbl_7, tbl_8, tbl_9, tbl_10, tbl_11, tbl_12, tbl_13, tbl_14, tbl_15, tbl_16, tbl_17, tbl_18, tbl_19, tbl_20, tbl_21, tbl_22, tbl_23, tbl_24, tbl_25, tbl_26, W_top1, b_top1, W_top2, b_top2, W_top3 = _rec_inputs()

    def _L0_rec_setup():
        import jax, jax.numpy as jnp
        import numpy as np

        def _tri_indices(num_feas):
            return np.array([i * num_feas + j for j in range(1, num_feas) for i in range(j)], dtype=np.int32)
        key = jax.random.key(seed)
        batch, num_feas, embed_dim = (2048, 27, 128)
        inputs = jax.random.normal(key, (batch, num_feas, embed_dim), dtype=jnp.float32)
        return {'inputs': inputs, 'num_feas': num_feas}
    _L0_rec_all = _L0_rec_setup()
    _L0_rec_in = {k: v for k, v in _L0_rec_all.items() if k in ()}
    del _L0_rec_all
    return {'dense_ctx': dense_ctx, 'ids': ids, 'tbl_0': tbl_0, 'tbl_1': tbl_1, 'tbl_2': tbl_2, 'tbl_3': tbl_3, 'tbl_4': tbl_4, 'tbl_5': tbl_5, 'tbl_6': tbl_6, 'tbl_7': tbl_7, 'tbl_8': tbl_8, 'tbl_9': tbl_9, 'tbl_10': tbl_10, 'tbl_11': tbl_11, 'tbl_12': tbl_12, 'tbl_13': tbl_13, 'tbl_14': tbl_14, 'tbl_15': tbl_15, 'tbl_16': tbl_16, 'tbl_17': tbl_17, 'tbl_18': tbl_18, 'tbl_19': tbl_19, 'tbl_20': tbl_20, 'tbl_21': tbl_21, 'tbl_22': tbl_22, 'tbl_23': tbl_23, 'tbl_24': tbl_24, 'tbl_25': tbl_25, 'tbl_26': tbl_26, 'W_top1': W_top1, 'b_top1': b_top1, 'W_top2': W_top2, 'b_top2': b_top2, 'W_top3': W_top3}

def reference(dense_ctx, ids, tbl_0, tbl_1, tbl_2, tbl_3, tbl_4, tbl_5, tbl_6, tbl_7, tbl_8, tbl_9, tbl_10, tbl_11, tbl_12, tbl_13, tbl_14, tbl_15, tbl_16, tbl_17, tbl_18, tbl_19, tbl_20, tbl_21, tbl_22, tbl_23, tbl_24, tbl_25, tbl_26, W_top1, b_top1, W_top2, b_top2, W_top3):
    import jax
    import jax.numpy as jnp

    def _L0_rec_ref(inputs, num_feas):
        import jax, jax.numpy as jnp
        import numpy as np

        def _tri_indices(num_feas):
            return np.array([i * num_feas + j for j in range(1, num_feas) for i in range(j)], dtype=np.int32)
        dot = jnp.einsum('bnd,bmd->bnm', inputs, inputs)
        idx = jnp.asarray(_tri_indices(num_feas))
        flat = dot.reshape(inputs.shape[0], num_feas * num_feas)
        return flat[:, idx]
    e = jnp.stack([tbl_0[ids[:, 0]], tbl_1[ids[:, 1]], tbl_2[ids[:, 2]], tbl_3[ids[:, 3]], tbl_4[ids[:, 4]], tbl_5[ids[:, 5]], tbl_6[ids[:, 6]], tbl_7[ids[:, 7]], tbl_8[ids[:, 8]], tbl_9[ids[:, 9]], tbl_10[ids[:, 10]], tbl_11[ids[:, 11]], tbl_12[ids[:, 12]], tbl_13[ids[:, 13]], tbl_14[ids[:, 14]], tbl_15[ids[:, 15]], tbl_16[ids[:, 16]], tbl_17[ids[:, 17]], tbl_18[ids[:, 18]], tbl_19[ids[:, 19]], tbl_20[ids[:, 20]], tbl_21[ids[:, 21]], tbl_22[ids[:, 22]], tbl_23[ids[:, 23]], tbl_24[ids[:, 24]], tbl_25[ids[:, 25]], tbl_26[ids[:, 26]]], axis=1)
    z = _L0_rec_ref(e, 27)
    z = z.reshape(z.shape[0], -1)
    h = jnp.concatenate([z, dense_ctx], axis=1)
    h = jnp.maximum(h @ W_top1 + b_top1, 0.0)
    h = jnp.maximum(h @ W_top2 + b_top2, 0.0)
    y = h @ W_top3
    return y

_drawn_inputs = setup_inputs


def setup_inputs(seed=0):
    import zlib

    import numpy as np

    out = dict(_drawn_inputs(seed))
    spreads = {'b_top1': (0.0, 0.1), 'b_top2': (0.0, 0.1)}
    factors = {}
    for name, (base, spread) in spreads.items():
        noise = np.random.default_rng([zlib.crc32(name.encode()), seed]).standard_normal(out[name].shape)
        drawn = base * np.exp(spread * noise) if base else spread * noise
        out[name] = jnp.asarray(drawn.astype(out[name].dtype))
    for name, factor in factors.items():
        out[name] = (out[name] * factor).astype(out[name].dtype)
    return out
```

```python
import concourse.bass as bass
from concourse import mybir
from contextlib import ExitStack

BATCH, FEATS, DIM, DENSE = 512, 27, 128, 16
H1, H2 = 512, 256
P = 128
TILES = BATCH // P
SLOT = 32
CLASSES = P // SLOT
GROUPS = P // CLASSES
QUAD = 4
QUADS = -(-FEATS // QUAD)
QCOUNT = [min(QUAD, FEATS - QUAD * k) for k in range(QUADS)]
JQ = 7
PAIRS = FEATS * (FEATS - 1) // 2
BLOCK = CLASSES * FEATS
PER_BANK = 4
UNIT = 2 * PER_BANK
UNITS = GROUPS // UNIT
C1, C2 = H1 // P, H2 // P


def program(nc, ids, tables, dense, w1, b1, w2, b2, w3, y):
    fp32, i32 = mybir.dt.float32, mybir.dt.int32
    ALU, ACT = mybir.AluOpType, mybir.ActivationFunctionType
    with ExitStack() as ctx:
        def sb(name, shape, dt=fp32):
            return ctx.enter_context(nc.sbuf_tensor(name, shape, dt))

        def ps(name, shape):
            return ctx.enter_context(nc.psum_tensor(name, shape, fp32))

        def sem(name):
            return ctx.enter_context(nc.semaphore(name))

        ids_sb = sb("ids_sb", [P, TILES, FEATS], i32)
        rows = sb("rows", [P, FEATS, DIM])
        emb = sb("emb", [P, GROUPS, CLASSES, SLOT])
        pairs = sb("pairs", [P, JQ, P])
        w1_sb = sb("w1_sb", [P, JQ, H1])
        w2_sb = sb("w2_sb", [P, C1, H2])
        w3_sb = sb("w3_sb", [P, C2])
        b1_sb = sb("b1_sb", [P, C1])
        b2_sb = sb("b2_sb", [P, C2])
        dense_wide = sb("dense_wide", [P, TILES, P])
        dense_t = sb("dense_t", [P, BATCH])
        ident = sb("ident", [P, P])
        hid1 = sb("hid1", [P, C1, P])
        hid2 = sb("hid2", [P, C2, P])
        y_sb = sb("y_sb", [1, BATCH])

        turn_ps = ps("turn_ps", [P, 2, QUAD, P])
        gram_ps = ps("gram_ps", [P, 2, 2, 512])
        mlp_ps = ps("mlp_ps", [P, 2, 512])
        hid1_ps = [mlp_ps[:, c // 2, (c % 2) * P:(c % 2 + 1) * P] for c in range(C1)]
        hid2_ps = [mlp_ps[:, c, 2 * P:3 * P] for c in range(C2)]
        y_ps = mlp_ps[0:1, 0, 3 * P:4 * P]

        ids_in = sem("ids_in")
        dense_in = sem("dense_in")
        weights_in = sem("weights_in")
        rows_in = [sem(f"rows_in{k}") for k in range(QUADS)]
        ident_zeroed = sem("ident_zeroed")
        ident_ready = sem("ident_ready")
        dense_zeroed = sem("dense_zeroed")
        w1_zeroed = sem("w1_zeroed")
        pads_zeroed = sem("pads_zeroed")
        dense_turned = sem("dense_turned")
        turned = sem("turned")
        emb_even = sem("emb_even")
        emb_odd = sem("emb_odd")
        gram_done = sem("gram_done")
        unpacked_v = sem("unpacked_v")
        unpacked_s = sem("unpacked_s")
        hid1_summed = sem("hid1_summed")
        hid1_ready_v = sem("hid1_ready_v")
        hid1_ready_s = sem("hid1_ready_s")
        hid2_summed = sem("hid2_summed")
        hid2_ready_v = sem("hid2_ready_v")
        hid2_ready_s = sem("hid2_ready_s")
        y_summed = sem("y_summed")
        mlp_ps_copied = sem("mlp_ps_copied")
        y_out = sem("y_out")
        block = ctx.enter_context(nc.Block())

        EVEN = (QUADS + 1) // 2
        ODD = QUADS // 2
        tri = [j * (j - 1) // 2 for j in range(FEATS + 1)]
        N_WEIGHTS = 16 * ((FEATS - 1) + 1 + 4)

        pairs_by_unit = pairs[:].rearrange("p q (c u m) -> p c u q m", c=CLASSES, u=UNITS)
        w1_cols = w1_sb[:].rearrange("p q (o c) -> p q c o", c=C1)
        w2_cols = w2_sb[:].rearrange("p k (o c) -> p k c o", c=C2)

        def gram_slice(u, half):
            return gram_ps[:, u % 2, half, 0:PER_BANK * BLOCK].rearrange("p (m n) -> p m n", m=PER_BANK)

        def unpack(copy, u, c):
            for g in range(4):
                nq = len(range(g, FEATS, 4))
                src = gram_ps[SLOT * c:SLOT * (c + 1), u % 2, :, 0:PER_BANK * BLOCK].rearrange(
                    "p b (m n) -> p b m n", m=PER_BANK)[:, :, :, FEATS * c + g:FEATS * c + g + 4 * (nq - 1) + 1:4]
                dst = pairs_by_unit[SLOT * g:SLOT * (g + 1), c, u, 0:nq, :].rearrange(
                    "p q (b m) -> p b m q", b=2)
                last = copy(dst, src)
            return last

        @block.sync
        def _(sp):
            sp.dma_start(ids_sb[:], ids.rearrange("(t p) f -> p t f", p=P)).then_inc(ids_in, 16)
            sp.wait_ge(dense_zeroed, 1)
            sp.dma_start(dense_wide[:, :, 96:96 + DENSE], dense.rearrange("(t p) f -> p t f", p=P)).then_inc(dense_in, 16)
            sp.wait_ge(w1_zeroed, 1)
            for j in range(1, FEATS):
                g = SLOT * (j % 4)
                sp.dma_start(w1_sb[g:g + j, j // 4, :], w1[tri[j]:tri[j + 1], :]).then_inc(weights_in, 16)
            sp.dma_start(w1_sb[96:96 + DENSE, JQ - 1, :], w1[PAIRS:PAIRS + DENSE, :]).then_inc(weights_in, 16)
            sp.dma_start(w2_sb[:], w2.rearrange("(p c) n -> p c n", c=C1)).then_inc(weights_in, 16)
            sp.dma_start(w3_sb[:], w3.rearrange("(p c) o -> p (c o)", c=C2)).then_inc(weights_in, 16)
            sp.dma_start(b1_sb[:], b1.rearrange("(p c) -> p c", c=C1)).then_inc(weights_in, 16)
            sp.dma_start(b2_sb[:], b2.rearrange("(p c) -> p c", c=C2)).then_inc(weights_in, 16)
            sp.wait_ge(mlp_ps_copied, 1 + TILES)
            sp.dma_start(y.rearrange("b o -> o b"), y_sb[:]).then_inc(y_out, 16)
            sp.wait_ge(y_out, 16)

        @block.gpsimd
        def _(pool):
            nc.gpsimd.memset(ident[:], 0.0).then_inc(ident_zeroed, 1)
            pool.wait_ge(ident_zeroed, 1)
            nc.gpsimd.affine_select(out=ident[:], in_=ident[:], compare_op=ALU.not_equal, fill=1.0, base=0,
                                    pattern=[[-1, P]], channel_multiplier=1).then_inc(ident_ready, 1)
            pool.wait_ge(ids_in, 16)

            for t in range(TILES):
                for f in range(FEATS):
                    k = f // QUAD
                    if t > 0 and f % QUAD == 0:
                        pool.wait_ge(turned, (t - 1) * QUADS + k + 1)
                    nc.gpsimd.indirect_dma_start(
                        out=rows[:, f, :], out_offset=None, in_=tables[f],
                        in_offset=bass.IndirectOffsetOnAxis(ap=ids_sb[:, t, f:f + 1], axis=0),
                    ).then_inc(rows_in[k], 16)

        @block.tensor
        def _(pe):
            pe.wait_ge(ident_ready, 1)
            pe.wait_ge(dense_in, 16)
            for t in range(TILES):
                last = nc.tensor.transpose(mlp_ps[:, 0, t * P:(t + 1) * P], dense_wide[:, t, :], ident[:])
            last.then_inc(dense_turned, 1)
            pe.wait_ge(pads_zeroed, 1)
            with pe.Fori(0, TILES) as t:
                for k in range(QUADS):
                    pe.wait_ge(rows_in[k], (t + 1) * (16 * QCOUNT[k]))
                    if k < 2:
                        pass
                    elif k % 2 == 0:
                        pe.wait_ge(emb_even, t * EVEN + k // 2)
                    else:
                        pe.wait_ge(emb_odd, t * ODD + k // 2)
                    for m in range(QCOUNT[k]):
                        last = nc.tensor.transpose(turn_ps[:, k % 2, m, :], rows[:, QUAD * k + m, :], ident[:])
                    last.then_inc(turned, 1)
                pe.wait_ge(emb_even, (t + 1) * EVEN)
                pe.wait_ge(emb_odd, (t + 1) * ODD)
                for u in range(UNITS):
                    if u >= 2:
                        pe.wait_ge(unpacked_v, t * UNITS + (u - 1))
                        pe.wait_ge(unpacked_s, t * UNITS + (u - 1))
                    for m in range(UNIT):
                        r = u * UNIT + m
                        last = nc.tensor.matmul(gram_slice(u, m // PER_BANK)[:, m % PER_BANK, :],
                                                emb[:, r, :, :].rearrange("d c f -> d (c f)"), emb[:, r, :, 0:FEATS],
                                                start=True, stop=True)
                    last.then_inc(gram_done, 1)
                pe.wait_ge(weights_in, N_WEIGHTS)
                pe.wait_ge(mlp_ps_copied, t + 1)
                pe.wait_ge(unpacked_v, (t + 1) * UNITS)
                pe.wait_ge(unpacked_s, (t + 1) * UNITS)
                for c in range(C1):
                    for q in range(JQ):
                        last = nc.tensor.matmul(hid1_ps[c], w1_cols[:, q, c, :], pairs[:, q, :],
                                                start=(q == 0), stop=(q == JQ - 1))
                    if c % 2 == 1:
                        last.then_inc(hid1_summed, 1)
                pe.wait_ge(hid1_ready_v, t + 1)
                pe.wait_ge(hid1_ready_s, t + 1)
                for c in range(C2):
                    for k in range(C1):
                        last = nc.tensor.matmul(hid2_ps[c], w2_cols[:, k, c, :], hid1[:, k, :],
                                                start=(k == 0), stop=(k == C1 - 1))
                    last.then_inc(hid2_summed, 1)
                pe.wait_ge(hid2_ready_v, t + 1)
                pe.wait_ge(hid2_ready_s, t + 1)
                for c in range(C2):
                    last = nc.tensor.matmul(y_ps, w3_sb[:, c:c + 1], hid2[:, c, :],
                                            start=(c == 0), stop=(c == C2 - 1))
                last.then_inc(y_summed, 1)

        def emb_quad(k):
            n = QCOUNT[k]
            return (emb[:, :, :, QUAD * k:QUAD * k + n].rearrange("d r c f -> d c r f"),
                    turn_ps[:, k % 2, 0:n, :].rearrange("d f (c r) -> d c r f", c=CLASSES))

        @block.vector
        def _(dve):
            nc.vector.memset(dense_wide[:], 0.0).then_inc(dense_zeroed, 1)
            nc.vector.memset(emb[:, :, :, FEATS:SLOT], 0.0).then_inc(pads_zeroed, 1)
            nc.vector.memset(w1_sb[:], 0.0).then_inc(w1_zeroed, 1)
            dve.wait_ge(dense_turned, 1)
            nc.vector.tensor_copy(dense_t[96:128, :], mlp_ps[96:128, 0, :]).then_inc(mlp_ps_copied, 1)
            dve.wait_ge(mlp_ps_copied, 1)
            dve.wait_ge(weights_in, N_WEIGHTS)
            with dve.Fori(0, TILES) as t:
                for k in range(0, QUADS, 2):
                    dve.wait_ge(turned, t * QUADS + (k + 1))
                    dst, src = emb_quad(k)
                    nc.vector.tensor_copy(dst, src).then_inc(emb_even, 1)
                nc.vector.tensor_copy(pairs[96:128, JQ - 1, :], dense_t[96:128, bass.ds(t * P, P)])
                for u in range(UNITS):
                    dve.wait_ge(gram_done, t * UNITS + (u + 1))
                    unpack(nc.vector.tensor_copy, u, 0)
                    unpack(nc.vector.tensor_copy, u, 1).then_inc(unpacked_v, 1)
                dve.wait_ge(hid1_summed, t * 2 + 1)
                for c in (0, 1):
                    last = nc.vector.tensor_scalar(hid1[:, c, :], hid1_ps[c], b1_sb[:, c:c + 1], 0.0,
                                                   ALU.add, ALU.max)
                last.then_inc(hid1_ready_v, 1)
                dve.wait_ge(hid2_summed, t * C2 + 1)
                nc.vector.tensor_scalar(hid2[:, 0, :], hid2_ps[0], b2_sb[:, 0:1], 0.0,
                                        ALU.add, ALU.max).then_inc(hid2_ready_v, 1)
                dve.wait_ge(y_summed, t + 1)
                nc.vector.tensor_copy(y_sb[:, bass.ds(t * P, P)], y_ps).then_inc(mlp_ps_copied, 1)

        @block.scalar
        def _(act):
            act.wait_ge(weights_in, N_WEIGHTS)
            with act.Fori(0, TILES) as t:
                for k in range(1, QUADS, 2):
                    act.wait_ge(turned, t * QUADS + (k + 1))
                    dst, src = emb_quad(k)
                    nc.scalar.copy(dst, src).then_inc(emb_odd, 1)
                for u in range(UNITS):
                    act.wait_ge(gram_done, t * UNITS + (u + 1))
                    unpack(nc.scalar.copy, u, 2)
                    unpack(nc.scalar.copy, u, 3).then_inc(unpacked_s, 1)
                act.wait_ge(hid1_summed, t * 2 + 2)
                for c in (2, 3):
                    last = nc.scalar.activation(hid1[:, c, :], hid1_ps[c], ACT.Relu, bias=b1_sb[:, c:c + 1])
                last.then_inc(hid1_ready_s, 1)
                act.wait_ge(hid2_summed, t * C2 + 2)
                nc.scalar.activation(hid2[:, 1, :], hid2_ps[1], ACT.Relu, bias=b2_sb[:, 1:2]).then_inc(hid2_ready_s, 1)


def kernel(**inputs):
    import numpy as _np
    import concourse.bacc as _bacc
    from concourse.bass_utils import run_bass_kernel_spmd as _run
    nc = _bacc.Bacc("TRN2", target_bir_lowering=False, num_devices=1)
    arrays, aps = {}, {}
    for name, value in inputs.items():
        a = _np.ascontiguousarray(value)
        arrays[f"in_{name}"] = a
        aps[name] = nc.dram_tensor(f"in_{name}", a.shape, mybir.dt.from_np(a.dtype), kind="ExternalInput").ap()
    y = nc.dram_tensor("y", (BATCH, 1), mybir.dt.float32, kind="ExternalOutput").ap()
    program(nc, aps["ids"], [aps[f"tbl_{f}"] for f in range(FEATS)], aps["dense_ctx"],
            aps["W_top1"], aps["b_top1"], aps["W_top2"], aps["b_top2"], aps["W_top3"], y)
    return _run(nc, [arrays], core_ids=[0]).results[0]["y"]
```

```python
import concourse.bass as bass
from concourse import mybir
from contextlib import ExitStack

BATCH, FEATS, DIM, DENSE = 512, 27, 128, 16
H1, H2 = 512, 256
P = 128
TILES = BATCH // P
SLOT = 32
CLASSES = P // SLOT
GROUPS = P // CLASSES
ONEHOT = 7
SMALL = [7, 10, 13, 14, 18, 19, 20, 21, 22, 23, 24, 25, 26]
VOCAB = 1000
GATHERED = FEATS - ONEHOT
SLOTS = SMALL[-ONEHOT:] + [f for f in range(FEATS) if f not in SMALL[-ONEHOT:]]
CHUNKS = 8
HALF = CHUNKS // 2
VP = VOCAB // CHUNKS
VP16 = VP // 16 * 16
LOOPED = (ONEHOT - 1) // 2 * 2
WARM_UP = 20
QUAD = 4
QUADS = -(-GATHERED // QUAD)
QCOUNT = [min(QUAD, GATHERED - QUAD * k) for k in range(QUADS)]
COLS = FEATS - 1
COLS_OF = [len(range(g, COLS, 4)) for g in range(4)]
ROWS = FEATS - 1
JQ = 7
DENSE_P = SLOT * (COLS % 4)
GRAM_P = (CLASSES - 1) * SLOT + ROWS
BLOCK = CLASSES * COLS
PER_BANK = 4
UNIT = 2 * PER_BANK
UNITS = GROUPS // UNIT
C1, C2 = H1 // P, H2 // P


def program(nc, ids, ids_t, tables, dense, w1, b1, w2, b2, w3, y):
    fp32, fp32r, i32 = mybir.dt.float32, mybir.dt.float32r, mybir.dt.int32
    ALU, ACT = mybir.AluOpType, mybir.ActivationFunctionType
    with ExitStack() as ctx:
        def sb(name, shape, dt=fp32):
            return ctx.enter_context(nc.sbuf_tensor(name, shape, dt))

        def ps(name, shape):
            return ctx.enter_context(nc.psum_tensor(name, shape, fp32))

        def sem(name):
            return ctx.enter_context(nc.semaphore(name))

        ids_sb = sb("ids_sb", [P, TILES, GATHERED], i32)
        ids_wide = sb("ids_wide", [P, ONEHOT, BATCH], i32)
        row_ids_i = sb("row_ids_i", [VP, CHUNKS], i32)
        row_ids = sb("row_ids", [VP, CHUNKS])
        minus_row_ids = sb("minus_row_ids", [VP, CHUNKS])
        one = sb("one", [P, 1])
        zero = sb("zero", [P, 1])
        table = sb("table", [VP, 2, CHUNKS, DIM])
        table_hi = sb("table_hi", [VP, 2, CHUNKS, DIM], fp32r)
        table_lo = sb("table_lo", [VP, 2, CHUNKS, DIM], fp32r)
        distance = sb("distance", [VP, 2, BATCH])
        onehot = sb("onehot", [VP, 2, HALF, BATCH], fp32r)
        rows = sb("rows", [P, 2, GATHERED, DIM])
        emb = sb("emb", [P, TILES, GROUPS, CLASSES, SLOT])
        pairs = sb("pairs", [P, JQ, P])
        w1_sb = sb("w1_sb", [P, C1, JQ, P])
        w2_sb = sb("w2_sb", [P, C1, H2])
        w3_sb = sb("w3_sb", [P, C2])
        b1_sb = sb("b1_sb", [P, C1])
        b2_sb = sb("b2_sb", [P, C2])
        dense_wide = sb("dense_wide", [P, TILES, P])
        dense_t = sb("dense_t", [P, BATCH])
        ident = sb("ident", [P, P])
        hid1 = sb("hid1", [P, C1, P])
        hid2 = sb("hid2", [P, C2, P])
        y_sb = sb("y_sb", [1, BATCH])

        turn_ps = ps("turn_ps", [P, 2, QUAD, P])
        gram_ps = ps("gram_ps", [P, 2, 2, 512])
        mlp_ps = ps("mlp_ps", [P, 2, 512])
        hid1_ps = [mlp_ps[:, c // 2, (c % 2) * P:(c % 2 + 1) * P] for c in range(C1)]
        hid2_ps = [mlp_ps[:, c, 2 * P:3 * P] for c in range(C2)]
        y_ps = mlp_ps[0:1, 0, 3 * P:4 * P]

        ids_in = sem("ids_in")
        ids_wide_in = sem("ids_wide_in")
        ids_wide_rest_in = sem("ids_wide_rest_in")
        dense_in = sem("dense_in")
        table_in = [sem(f"table_in{h}") for h in range(2)]
        weights_in = sem("weights_in")
        rows_in = [[sem(f"rows_in{h}_{k}") for k in range(QUADS)] for h in range(2)]
        row_ids_made = sem("row_ids_made")
        row_ids_ready = sem("row_ids_ready")
        ident_zeroed = sem("ident_zeroed")
        ident_ready = sem("ident_ready")
        dense_zeroed = sem("dense_zeroed")
        constants_ready = sem("constants_ready")
        pads_zeroed = sem("pads_zeroed")
        dense_turned = sem("dense_turned")
        pairs_zeroed = sem("pairs_zeroed")
        hi_ready = sem("hi_ready")
        lo_ready = sem("lo_ready")
        distance_ready = sem("distance_ready")
        onehot_v = sem("onehot_v")
        onehot_s = sem("onehot_s")
        lookup_summed = sem("lookup_summed")
        lookup_copied = sem("lookup_copied")
        turned = sem("turned")
        emb_even = sem("emb_even")
        emb_odd = sem("emb_odd")
        gram_done = sem("gram_done")
        unpacked_v = sem("unpacked_v")
        unpacked_s = sem("unpacked_s")
        hid1_summed = sem("hid1_summed")
        hid1_ready_v = sem("hid1_ready_v")
        hid1_ready_s = sem("hid1_ready_s")
        hid2_summed = sem("hid2_summed")
        hid2_ready_v = sem("hid2_ready_v")
        hid2_ready_s = sem("hid2_ready_s")
        y_summed = sem("y_summed")
        mlp_ps_copied = sem("mlp_ps_copied")
        y_out = sem("y_out")
        block = ctx.enter_context(nc.Block())

        N_WEIGHTS = 16 * 5
        pairs_by_unit = pairs[:].rearrange("p q (c u m) -> p c u q m", c=CLASSES, u=UNITS)
        w2_cols = w2_sb[:].rearrange("p k (o c) -> p k c o", c=C2)

        def unpack(copy, u, c):
            for g in range(4):
                n = COLS_OF[g]
                src = gram_ps[SLOT * c:SLOT * c + ROWS, u % 2, :, 0:PER_BANK * BLOCK].rearrange(
                    "p b (m n) -> p b m n", m=PER_BANK)[:, :, :, COLS * c + g:COLS * c + g + 4 * (n - 1) + 1:4]
                dst = pairs_by_unit[SLOT * g:SLOT * g + ROWS, c, u, 0:n, :].rearrange("p q (b m) -> p b m q", b=2)
                last = copy(dst, src)
            return last

        def copy_quad(copy, t, k):
            s0 = ONEHOT + QUAD * k
            return copy(emb[:, t, :, :, s0:s0 + QCOUNT[k]].rearrange("d r c f -> d c r f"),
                        turn_ps[:, (t * QUADS + k) % 2, 0:QCOUNT[k], :].rearrange("d f (c r) -> d c r f", c=CLASSES))

        @block.sync
        def _(sp):
            sp.dma_start(ids_sb[:], ids.rearrange("(t p) f -> p t f", p=P)).then_inc(ids_in, 16)

            def load_table(x):
                h = x % 2
                if x >= 2:
                    sp.wait_ge(hi_ready, x - 1)
                    sp.wait_ge(lo_ready, x - 1)
                rows_of = tables[SLOTS[x]].rearrange("(p c) d -> p c d", c=CHUNKS)
                sp.dma_start(table[0:VP16, h], rows_of[0:VP16]).then_inc(table_in[h], 16)
                sp.dma_start(table[VP16:VP, h], rows_of[VP16:VP]).then_inc(table_in[h], 16)

            load_table(0)
            sp.dma_start(ids_wide[:, 0:2, :].rearrange("p f b -> p (f b)"),
                         ids_t[0:2, :].rearrange("f b -> (f b)")
                         .partition_broadcast(P)).then_inc(ids_wide_in, 16)
            sp.wait_ge(dense_zeroed, 1)
            sp.dma_start(dense_wide[:, :, DENSE_P:DENSE_P + DENSE],
                         dense.rearrange("(t p) f -> p t f", p=P)).then_inc(dense_in, 16)
            load_table(1)
            sp.dma_start(ids_wide[:, 2:ONEHOT, :].rearrange("p f b -> p (f b)"),
                         ids_t[2:ONEHOT, :].rearrange("f b -> (f b)")
                         .partition_broadcast(P)).then_inc(ids_wide_rest_in, 16)
            for x in range(2, ONEHOT):
                load_table(x)
            sp.dma_start(w1_sb[:], w1).then_inc(weights_in, 16)
            sp.dma_start(w2_sb[:], w2.rearrange("(p c) n -> p c n", c=C1)).then_inc(weights_in, 16)
            sp.dma_start(w3_sb[:], w3.rearrange("(p c) o -> p (c o)", c=C2)).then_inc(weights_in, 16)
            sp.dma_start(b1_sb[:], b1.rearrange("(p c) -> p c", c=C1)).then_inc(weights_in, 16)
            sp.dma_start(b2_sb[:], b2.rearrange("(p c) -> p c", c=C2)).then_inc(weights_in, 16)
            sp.wait_ge(mlp_ps_copied, 1 + TILES)
            sp.dma_start(y.rearrange("b o -> o b"), y_sb[:]).then_inc(y_out, 16)
            sp.wait_ge(y_out, 16)

        @block.gpsimd
        def _(pool):
            nc.gpsimd.iota(row_ids_i[:], pattern=[[1, CHUNKS]], base=0, channel_multiplier=CHUNKS).then_inc(row_ids_made, 1)
            nc.gpsimd.memset(ident[:], 0.0).then_inc(ident_zeroed, 1)
            pool.wait_ge(ident_zeroed, 1)
            nc.gpsimd.affine_select(out=ident[:], in_=ident[:], compare_op=ALU.not_equal, fill=1.0, base=0,
                                    pattern=[[-1, P]], channel_multiplier=1).then_inc(ident_ready, 1)
            pool.wait_ge(ids_in, 16)
            for t in range(TILES):
                for f in range(GATHERED):
                    k = f // QUAD
                    if t >= 2 and f % QUAD == 0:
                        pool.wait_ge(turned, (t - 2) * QUADS + k + 1)
                    nc.gpsimd.indirect_dma_start(
                        out=rows[:, t % 2, f, :], out_offset=None, in_=tables[SLOTS[ONEHOT + f]],
                        in_offset=bass.IndirectOffsetOnAxis(ap=ids_sb[:, t, f:f + 1], axis=0),
                    ).then_inc(rows_in[t % 2][k], 16)

        @block.tensor
        def _(pe):
            pe.wait_ge(ident_ready, 1)
            for _ in range(WARM_UP):
                nc.tensor.transpose(mlp_ps[:, 1, 0:P], ident[:], ident[:])
            pe.wait_ge(dense_in, 16)
            for t in range(TILES):
                last = nc.tensor.transpose(mlp_ps[:, 0, t * P:(t + 1) * P], dense_wide[:, t, :], ident[:])
            last.then_inc(dense_turned, 1)

            def look_up(x, h, peeled):
                sums = gram_ps[:, h, 0, :]
                pe.wait_ge(hi_ready, x + 1)
                if not peeled:
                    pe.wait_ge(lookup_copied, x - 1)
                for half in range(2):
                    pe.wait_ge(onehot_v, 2 * x + (half + 1))
                    pe.wait_ge(onehot_s, 2 * x + (half + 1))
                    for part in (table_hi, table_lo):
                        if half == 0 and part is table_lo:
                            pe.wait_ge(lo_ready, x + 1)
                        for c in range(HALF):
                            last = nc.tensor.matmul(sums, part[:, h, half * HALF + c, :], onehot[:, half, c, :],
                                                    start=(half == 0 and c == 0 and part is table_hi),
                                                    stop=(half == 1 and c == HALF - 1 and part is table_lo))
                    last.then_inc(lookup_summed, 1)

            def turn(t, k):
                n = t * QUADS + k
                pe.wait_ge(rows_in[t % 2][k], (t // 2 + 1) * 16 * QCOUNT[k])
                if n >= 2:
                    pe.wait_ge(emb_odd if n % 2 else emb_even, n // 2)
                for m in range(QCOUNT[k]):
                    last = nc.tensor.transpose(turn_ps[:, n % 2, m, :], rows[:, t % 2, QUAD * k + m, :], ident[:])
                last.then_inc(turned, 1)

            def gram(t):
                pe.wait_ge(emb_even, ((t + 1) * QUADS + 1) // 2)
                pe.wait_ge(emb_odd, (t + 1) * QUADS // 2)
                for u in range(UNITS):
                    n = t * UNITS + u
                    if n >= 2:
                        pe.wait_ge(unpacked_v, n - 1)
                        pe.wait_ge(unpacked_s, n - 1)
                    for m in range(UNIT):
                        r = u * UNIT + m
                        out = gram_ps[0:GRAM_P, u % 2, m // PER_BANK, (m % PER_BANK) * BLOCK:(m % PER_BANK + 1) * BLOCK]
                        last = nc.tensor.matmul(out, emb[:, t, r, :, :].rearrange("d c f -> d (c f)")[:, 0:GRAM_P],
                                                emb[:, t, r, :, 1:FEATS], start=True, stop=True)
                    last.then_inc(gram_done, 1)

            def layer1(t, c):
                if c == 0:
                    pe.wait_ge(unpacked_v, (t + 1) * UNITS)
                    pe.wait_ge(unpacked_s, (t + 1) * UNITS)
                    if t == 0:
                        pe.wait_ge(mlp_ps_copied, 1)
                    else:
                        pe.wait_ge(hid2_ready_v, t)
                if c == 2 and t > 0:
                    pe.wait_ge(hid2_ready_s, t)
                if t == 0 and c == 0:
                    pe.wait_ge(weights_in, N_WEIGHTS)
                for q in range(JQ):
                    last = nc.tensor.matmul(hid1_ps[c], w1_sb[:, c, q, :], pairs[:, q, :],
                                            start=(q == 0), stop=(q == JQ - 1))
                if c % 2 == 1:
                    last.then_inc(hid1_summed, 1)

            def layer2(t):
                pe.wait_ge(hid1_ready_v, t + 1)
                pe.wait_ge(hid1_ready_s, t + 1)
                for c in (1, 0):
                    if c == 0:
                        pe.wait_ge(mlp_ps_copied, t + 1)
                    for k in range(C1):
                        last = nc.tensor.matmul(hid2_ps[c], w2_cols[:, k, c, :], hid1[:, k, :],
                                                start=(k == 0), stop=(k == C1 - 1))
                    last.then_inc(hid2_summed, 1)

            def layer3(t):
                pe.wait_ge(hid2_ready_v, t + 1)
                pe.wait_ge(hid2_ready_s, t + 1)
                if t + 1 < TILES:
                    pe.wait_ge(hid1_ready_v, t + 2)
                for c in range(C2):
                    last = nc.tensor.matmul(y_ps, w3_sb[:, c:c + 1], hid2[:, c, :],
                                            start=(c == 0), stop=(c == C2 - 1))
                last.then_inc(y_summed, 1)

            look_up(0, 0, True)
            look_up(1, 1, True)
            with pe.Fori(1, LOOPED // 2) as i:
                look_up(2 * i, 0, False)
                look_up(2 * i + 1, 1, False)
            for x in range(LOOPED, ONEHOT - 1):
                look_up(x, x % 2, False)
            turn(0, 0)
            turn(0, 1)
            look_up(ONEHOT - 1, (ONEHOT - 1) % 2, False)
            for k in range(2, QUADS):
                turn(0, k)
            pe.wait_ge(lookup_copied, ONEHOT)
            pe.wait_ge(pads_zeroed, 1)
            for t in range(TILES):
                gram(t)
                if t > 0:
                    layer2(t - 1)
                if t + 1 < TILES:
                    turn(t + 1, 0)
                    turn(t + 1, 1)
                for c in range(C1):
                    layer1(t, c)
                    if t + 1 < TILES and c + 2 < QUADS:
                        turn(t + 1, c + 2)
                if t > 0:
                    layer3(t - 1)
            layer2(TILES - 1)
            layer3(TILES - 1)

        @block.vector
        def _(dve):
            nc.vector.memset(dense_wide[:], 0.0).then_inc(dense_zeroed, 1)
            nc.vector.memset(one[:], 1.0)
            nc.vector.memset(zero[:], 0.0).then_inc(constants_ready, 1)
            dve.wait_ge(row_ids_made, 1)
            nc.vector.tensor_copy(row_ids[:], row_ids_i[:])
            nc.vector.tensor_scalar(minus_row_ids[:], row_ids_i[:], -1.0, None, ALU.mult).then_inc(row_ids_ready, 1)
            dve.wait_ge(row_ids_ready, 1)
            dve.wait_ge(ids_wide_in, 16)

            def operands(x, h, peeled, very_first=False):
                ids_x = ids_wide[0:VP, bass.ds(x, 1), :].rearrange("p a b -> p (a b)")
                for half in range(2):
                    if not very_first:
                        dve.wait_ge(lookup_summed, 2 * x + (half - 1))
                    for c in range(HALF - 1):
                        row = half * HALF + c
                        last = nc.vector.tensor_scalar(onehot[:, half, c, :], ids_x, row_ids[:, row:row + 1], None, ALU.is_equal)
                    last.then_inc(onehot_v, 1)
                    if half == 0:
                        dve.wait_ge(hi_ready, x + 1)
                        nc.vector.tensor_tensor(table_lo[:, h], table[:, h], table_hi[:, h].bitcast(fp32),
                                                ALU.subtract).then_inc(lo_ready, 1)

            def quads(t, a, b):
                for k in range(a, b):
                    if (t * QUADS + k) % 2 == 0:
                        dve.wait_ge(turned, t * QUADS + k + 1)
                        copy_quad(nc.vector.tensor_copy, t, k).then_inc(emb_even, 1)

            def relu2(t):
                dve.wait_ge(hid2_summed, C2 * (t + 1))
                nc.vector.tensor_scalar(hid2[:, 0, :], hid2_ps[0], b2_sb[:, 0:1], 0.0,
                                        ALU.add, ALU.max).then_inc(hid2_ready_v, 1)

            def copy_y(t):
                dve.wait_ge(y_summed, t + 1)
                nc.vector.tensor_copy(y_sb[:, t * P:(t + 1) * P], y_ps).then_inc(mlp_ps_copied, 1)

            operands(0, 0, True, very_first=True)
            operands(1, 1, True)
            dve.wait_ge(dense_turned, 1)
            nc.vector.tensor_copy(dense_t[64:128, :], mlp_ps[64:128, 0, :]).then_inc(mlp_ps_copied, 1)
            nc.vector.memset(pairs[:], 0.0).then_inc(pairs_zeroed, 1)
            dve.wait_ge(ids_wide_rest_in, 16)
            with dve.Fori(1, LOOPED // 2) as i:
                operands(2 * i, 0, False)
                operands(2 * i + 1, 1, False)
            for x in range(LOOPED, ONEHOT):
                operands(x, x % 2, False)
            quads(0, 0, QUADS)
            dve.wait_ge(weights_in, N_WEIGHTS)
            dve.wait_ge(pairs_zeroed, 1)
            for t in range(TILES):
                for u in range(UNITS):
                    dve.wait_ge(gram_done, t * UNITS + u + 1)
                    unpack(nc.vector.tensor_copy, u, 0)
                    unpack(nc.vector.tensor_copy, u, 1).then_inc(unpacked_v, 1)
                if t > 0:
                    relu2(t - 1)
                if t + 1 < TILES:
                    quads(t + 1, 0, 3)
                dve.wait_ge(hid1_summed, 2 * t + 1)
                for c in (0, 1):
                    last = nc.vector.tensor_scalar(hid1[:, c, :], hid1_ps[c], b1_sb[:, c:c + 1], 0.0, ALU.add, ALU.max)
                last.then_inc(hid1_ready_v, 1)
                if t + 1 < TILES:
                    quads(t + 1, 3, QUADS)
                if t > 0:
                    copy_y(t - 1)
            relu2(TILES - 1)
            copy_y(TILES - 1)

        @block.scalar
        def _(act):
            act.wait_ge(constants_ready, 1)
            pads = emb[:].rearrange("d t r c f -> d (t r c) f")[:, :, FEATS:SLOT]
            nc.scalar.copy(pads, zero[:, 0:1].unsqueeze(2).to_broadcast([P, BATCH, SLOT - FEATS])).then_inc(pads_zeroed, 1)
            act.wait_ge(row_ids_ready, 1)
            act.wait_ge(ids_wide_in, 16)

            def operands(x, h, table_loads, very_first=False):
                act.wait_ge(table_in[h], table_loads)
                if not very_first:
                    act.wait_ge(onehot_s, 2 * x)
                nc.scalar.copy(table_hi[:, h], table[:, h]).then_inc(hi_ready, 1)
                ids_x = ids_wide[0:VP, bass.ds(x, 1), :].rearrange("p a b -> p (a b)")
                for half in range(2):
                    row = half * HALF + HALF - 1
                    nc.scalar.activation(distance[:, half], ids_x, ACT.Abs, bias=minus_row_ids[:, row:row + 1]).then_inc(distance_ready, 1)
                    if not very_first:
                        act.wait_ge(lookup_summed, 2 * x + (half - 1))
                    act.wait_ge(distance_ready, 2 * x + (half + 1))
                    nc.scalar.activation(onehot[:, half, HALF - 1, :], distance[:, half], ACT.Relu,
                                         bias=one[0:VP], scale=-1.0).then_inc(onehot_s, 1)
                if not very_first:
                    copy_sums(x - 1, 1 - h)

            def copy_sums(x, h):
                slot = emb[:, :, :, :, bass.ds(x, 1)].rearrange("d t r c f -> d t c (r f)")
                nc.scalar.copy(slot, gram_ps[:, h, 0, :].rearrange("d (t c r) -> d t c r", t=TILES, c=CLASSES)
                               ).then_inc(lookup_copied, 1)

            def quads(t, a, b):
                for k in range(a, b):
                    if (t * QUADS + k) % 2 == 1:
                        act.wait_ge(turned, t * QUADS + k + 1)
                        copy_quad(nc.scalar.copy, t, k).then_inc(emb_odd, 1)

            operands(0, 0, 32, very_first=True)
            operands(1, 1, 32)
            act.wait_ge(ids_wide_rest_in, 16)
            with act.Fori(1, LOOPED // 2) as i:
                operands(2 * i, 0, 32 * i + 32)
                operands(2 * i + 1, 1, 32 * i + 32)
            for x in range(LOOPED, ONEHOT):
                operands(x, x % 2, 32 * (x // 2 + 1))
            quads(0, 0, 2)
            act.wait_ge(lookup_summed, 2 * ONEHOT)
            copy_sums(ONEHOT - 1, (ONEHOT - 1) % 2)
            quads(0, 2, QUADS)
            act.wait_ge(weights_in, N_WEIGHTS)
            act.wait_ge(pairs_zeroed, 1)
            act.wait_ge(mlp_ps_copied, 1)
            for t in range(TILES):
                for u in range(UNITS):
                    act.wait_ge(gram_done, t * UNITS + u + 1)
                    if u == 0:
                        nc.scalar.copy(pairs[64:128, JQ - 1, :], dense_t[64:128, t * P:(t + 1) * P])
                    unpack(nc.scalar.copy, u, 2)
                    unpack(nc.scalar.copy, u, 3).then_inc(unpacked_s, 1)
                if t > 0:
                    act.wait_ge(hid2_summed, C2 * t - 1)
                    nc.scalar.activation(hid2[:, 1, :], hid2_ps[1], ACT.Relu, bias=b2_sb[:, 1:2]).then_inc(hid2_ready_s, 1)
                if t + 1 < TILES:
                    quads(t + 1, 0, QUADS)
                act.wait_ge(hid1_summed, 2 * t + 2)
                for c in (2, 3):
                    last = nc.scalar.activation(hid1[:, c, :], hid1_ps[c], ACT.Relu, bias=b1_sb[:, c:c + 1])
                last.then_inc(hid1_ready_s, 1)
            act.wait_ge(hid2_summed, C2 * TILES - 1)
            nc.scalar.activation(hid2[:, 1, :], hid2_ps[1], ACT.Relu, bias=b2_sb[:, 1:2]).then_inc(hid2_ready_s, 1)


def kernel(**inputs):
    import numpy as np
    import concourse.bacc as bacc
    from concourse.bass_utils import run_bass_kernel_spmd

    arrays = {name: np.ascontiguousarray(value) for name, value in inputs.items()}
    w1 = arrays["W_top1"]
    laid = np.zeros((P, JQ, H1), w1.dtype)
    for j in range(1, FEATS):
        for i in range(j):
            a, b = sorted((SLOTS[i], SLOTS[j]))
            laid[SLOT * ((j - 1) % 4) + i, (j - 1) // 4] = w1[b * (b - 1) // 2 + a]
    laid[DENSE_P:DENSE_P + DENSE, JQ - 1] = w1[FEATS * (FEATS - 1) // 2:]
    arrays["W_top1"] = np.ascontiguousarray(laid.reshape(P, JQ, P, C1).transpose(0, 3, 1, 2))
    arrays["ids_t"] = np.ascontiguousarray(arrays["ids"].T[SLOTS[:ONEHOT]])
    arrays["ids"] = np.ascontiguousarray(arrays["ids"][:, SLOTS[ONEHOT:]])

    nc = bacc.Bacc("TRN2", target_bir_lowering=False, num_devices=1)
    aps = {name: nc.dram_tensor(f"in_{name}", a.shape, mybir.dt.from_np(a.dtype), kind="ExternalInput").ap()
           for name, a in arrays.items()}
    y = nc.dram_tensor("y", (BATCH, 1), mybir.dt.float32, kind="ExternalOutput").ap()
    program(nc, aps["ids"], aps["ids_t"], [aps[f"tbl_{f}"] for f in range(FEATS)], aps["dense_ctx"],
            aps["W_top1"], aps["b_top1"], aps["W_top2"], aps["b_top2"], aps["W_top3"], y)
    got = run_bass_kernel_spmd(nc, [{f"in_{name}": a for name, a in arrays.items()}], core_ids=[0])
    return got.results[0]["y"]
```

```python
import concourse.bass as bass
from concourse import mybir
from contextlib import ExitStack

BATCH, FEATS, DIM, DENSE = 512, 27, 128, 16
H1, H2 = 512, 256
P = 128
TILES = BATCH // P
SLOT = 32
CLASSES = P // SLOT
GROUPS = P // CLASSES
ONEHOT = 8
SMALL = [7, 10, 13, 14, 18, 19, 20, 21, 22, 23, 24, 25, 26]
VOCAB = 1000
GATHERED = FEATS - ONEHOT
SLOTS = [f for f in range(FEATS) if f not in SMALL[-ONEHOT:]] + SMALL[-ONEHOT:]
CHUNKS = 8
HALF = CHUNKS // 2
VP = VOCAB // CHUNKS
VP16 = VP // 16 * 16
PAIRS = ONEHOT // 2
WARM_UP = 21
QUAD = 4
QCOUNT = [QUAD] * ((GATHERED - 1) // QUAD) + [(GATHERED - 1) % QUAD] * ((GATHERED - 1) % QUAD > 0) + [1]
QUADS = len(QCOUNT)
QSTART = [sum(QCOUNT[:k]) for k in range(QUADS)]
HEADS, MIDS = 20, 6
LAST = HEADS + MIDS
COPIED = HEADS + 1
JQ = HEADS // 4
SHORT = HEADS // 2
UNDER = [(0, 0, JQ, HEADS, SLOT), (1, 0, 1, HEADS + JQ, SLOT)]
APART = [(g, 0, JQ, JQ * g, SLOT) for g in (2, 3)]
OVER_MIDS = [(g, 0, JQ, JQ * g, LAST) for g in (0, 1)]
OVER_HEAD = [(3, JQ - 2, 1, LAST, SHORT)]
DENSE_P = 3 * SLOT
BLOCK = CLASSES * FEATS
PER_BANK = 4
UNIT = 2 * PER_BANK
UNITS = GROUPS // UNIT
C1, C2 = H1 // P, H2 // P


def program(nc, ids, ids_t, tables, dense, w1, b1, w2, b2, w3, y):
    fp32, fp32r, i32 = mybir.dt.float32, mybir.dt.float32r, mybir.dt.int32
    ALU, ACT = mybir.AluOpType, mybir.ActivationFunctionType
    with ExitStack() as ctx:
        def sb(name, shape, dt=fp32):
            return ctx.enter_context(nc.sbuf_tensor(name, shape, dt))

        def ps(name, shape):
            return ctx.enter_context(nc.psum_tensor(name, shape, fp32))

        def sem(name):
            return ctx.enter_context(nc.semaphore(name))

        ids_sb = sb("ids_sb", [P, TILES, GATHERED], i32)
        ids_wide = sb("ids_wide", [P, ONEHOT, BATCH], i32)
        row_ids_i = sb("row_ids_i", [VP, CHUNKS], i32)
        row_ids = sb("row_ids", [VP, CHUNKS])
        minus_row_ids = sb("minus_row_ids", [VP, CHUNKS])
        table = sb("table", [VP, 2, CHUNKS, DIM])
        table_hi = sb("table_hi", [VP, 2, CHUNKS, DIM], fp32r)
        table_lo = sb("table_lo", [VP, 2, CHUNKS, DIM], fp32r)
        distance = sb("distance", [VP, 2, 2, BATCH])
        onehot = sb("onehot", [VP, 2, 2, HALF, BATCH], fp32r)
        rows = sb("rows", [P, 2, GATHERED, DIM])
        emb = sb("emb", [P, TILES, GROUPS, CLASSES, SLOT])
        pairs = sb("pairs", [P, JQ, P])
        w1_sb = sb("w1_sb", [P, C1, JQ, P])
        w2_sb = sb("w2_sb", [P, C1, H2])
        w3_sb = sb("w3_sb", [P, C2])
        b1_sb = sb("b1_sb", [P, C1])
        b2_sb = sb("b2_sb", [P, C2])
        dense_wide = sb("dense_wide", [P, TILES, P])
        dense_t = sb("dense_t", [P, BATCH])
        ident = sb("ident", [P, P])
        hid1 = sb("hid1", [P, C1, P])
        hid2 = sb("hid2", [P, C2, P])
        y_sb = sb("y_sb", [1, BATCH])

        turn_ps = ps("turn_ps", [P, 2, QUAD, P])
        gram_ps = ps("gram_ps", [P, 2, 2, 512])
        mlp_ps = ps("mlp_ps", [P, 2, 512])
        hid1_ps = [mlp_ps[:, c // 2, (c % 2) * P:(c % 2 + 1) * P] for c in range(C1)]
        hid2_ps = [mlp_ps[:, c, 2 * P:3 * P] for c in range(C2)]
        y_ps = mlp_ps[0:1, 1, 3 * P:4 * P]

        ids_in = sem("ids_in")
        ids_wide_in = [sem(f"ids_wide_in{x}") for x in range(2)]
        ids_pairs_in = sem("ids_pairs_in")
        dense_in = sem("dense_in")
        table_in = [sem(f"table_in{h}") for h in range(2)]
        weights_in = sem("weights_in")
        rows_in = [[sem(f"rows_in{h}_{k}") for k in range(QUADS)] for h in range(2)]
        row_ids_made = sem("row_ids_made")
        row_ids_ready = sem("row_ids_ready")
        minus_row_ids_ready = sem("minus_row_ids_ready")
        ident_zeroed = sem("ident_zeroed")
        ident_ready = sem("ident_ready")
        dense_zeroed = sem("dense_zeroed")
        dense_turned = sem("dense_turned")
        pairs_zeroed = sem("pairs_zeroed")
        hi_ready = sem("hi_ready")
        lo_ready = sem("lo_ready")
        distance_ready = sem("distance_ready")
        onehot_v = sem("onehot_v")
        onehot_s = sem("onehot_s")
        lookup_summed = sem("lookup_summed")
        mids_repeated = sem("mids_repeated")
        lookup_copied = sem("lookup_copied")
        turned = sem("turned")
        emb_even = sem("emb_even")
        emb_odd = sem("emb_odd")
        gram_done = sem("gram_done")
        under_v = sem("under_v")
        under_s = sem("under_s")
        apart_v = sem("apart_v")
        apart_s = sem("apart_s")
        unpacked_v = sem("unpacked_v")
        unpacked_s = sem("unpacked_s")
        hid1_summed = sem("hid1_summed")
        hid1_ready_v = sem("hid1_ready_v")
        hid1_ready_s = sem("hid1_ready_s")
        hid2_summed = sem("hid2_summed")
        hid2_ready_v = sem("hid2_ready_v")
        hid2_ready_s = sem("hid2_ready_s")
        y_summed = sem("y_summed")
        dense_copied = sem("dense_copied")
        y_copied = sem("y_copied")
        y_out = sem("y_out")
        block = ctx.enter_context(nc.Block())

        N_WEIGHTS = 16 * 5
        pairs_by_unit = pairs[:].rearrange("p q (c u m) -> p c u q m", c=CLASSES, u=UNITS)
        w2_cols = w2_sb[:].rearrange("p k (o c) -> p k c o", c=C2)

        def hid1_sums(t, c):
            if t < TILES - 1:
                return hid1_ps[c]
            return turn_ps[:, c, 0, :] if c < 2 else gram_ps[:, c - 2, 0, 0:P]

        def unpack(copy, u, classes, places):
            for c in classes:
                for g, q, n, slot, rows_n in places:
                    src = gram_ps[SLOT * c:SLOT * c + rows_n, u % 2, :, 0:PER_BANK * BLOCK].rearrange(
                        "p b (m n) -> p b m n", m=PER_BANK)[:, :, :, FEATS * c + slot:FEATS * c + slot + n]
                    dst = pairs_by_unit[SLOT * g:SLOT * g + rows_n, c, u, q:q + n, :].rearrange("p q (b m) -> p b m q", b=2)
                    last = copy(dst, src)
            return last

        def unpack_unit(eng, copy, t, u, classes, under_done, apart_done):
            n = t * UNITS + u + 1
            unpack(copy, u, classes, UNDER).then_inc(under_done, 1)
            unpack(copy, u, classes, APART).then_inc(apart_done, 1)
            eng.wait_ge(under_done, n)
            last = unpack(copy, u, classes, OVER_MIDS)
            eng.wait_ge(apart_done, n)
            last = unpack(copy, u, classes, OVER_HEAD)
            return last

        def copy_quad(copy, t, k):
            s0 = QSTART[k]
            return copy(emb[:, t, :, :, s0:s0 + QCOUNT[k]].rearrange("d r c f -> d c r f"),
                        turn_ps[:, (t * QUADS + k) % 2, 0:QCOUNT[k], :].rearrange("d f (c r) -> d c r f", c=CLASSES))

        def repeat_mids(copy, tiles):
            return copy(emb[:, tiles, :, :, FEATS:SLOT].rearrange("d t r c f -> d (t r c) f"),
                        emb[:, tiles, :, :, COPIED:LAST].rearrange("d t r c f -> d (t r c) f"))

        @block.sync
        def _(sp):
            sp.dma_start(ids_sb[:], ids.rearrange("(t p) f -> p t f", p=P)).then_inc(ids_in, 16)

            def load_ids_wide(x, n, landed):
                sp.dma_start(ids_wide[:, x:x + n, :].rearrange("p f b -> p (f b)"),
                             ids_t[x:x + n, :].rearrange("f b -> (f b)").partition_broadcast(P)).then_inc(landed, 16)

            def load_table(x):
                h = x % 2
                rows_of = tables[SLOTS[GATHERED + x]].rearrange("(p c) d -> p c d", c=CHUNKS)
                sp.dma_start(table[0:VP16, h], rows_of[0:VP16]).then_inc(table_in[h], 16)
                sp.dma_start(table[VP16:VP, h], rows_of[VP16:VP]).then_inc(table_in[h], 16)

            load_ids_wide(0, 1, ids_wide_in[0])
            load_table(0)
            sp.wait_ge(dense_zeroed, 1)
            sp.dma_start(dense_wide[:, :, DENSE_P:DENSE_P + DENSE],
                         dense.rearrange("(t p) f -> p t f", p=P)).then_inc(dense_in, 16)
            load_ids_wide(1, 1, ids_wide_in[1])
            load_table(1)
            load_ids_wide(2, 2, ids_pairs_in)
            for x in range(2, ONEHOT):
                if x % 2 == 0 and x >= 4:
                    sp.wait_ge(onehot_v, 2 * x - 3)
                    sp.wait_ge(distance_ready, x + 1)
                    load_ids_wide(x, 2, ids_pairs_in)
                sp.wait_ge(hi_ready, x - 1)
                sp.wait_ge(lo_ready, x - 1)
                load_table(x)
            sp.dma_start(w1_sb[:], w1).then_inc(weights_in, 16)
            sp.dma_start(w2_sb[:], w2.rearrange("(p c) n -> p c n", c=C1)).then_inc(weights_in, 16)
            sp.dma_start(w3_sb[:], w3.rearrange("(p c) o -> p (c o)", c=C2)).then_inc(weights_in, 16)
            sp.dma_start(b1_sb[:], b1.rearrange("(p c) -> p c", c=C1)).then_inc(weights_in, 16)
            sp.dma_start(b2_sb[:], b2.rearrange("(p c) -> p c", c=C2)).then_inc(weights_in, 16)
            sp.wait_ge(y_copied, TILES)
            sp.dma_start(y.rearrange("b o -> o b"), y_sb[:]).then_inc(y_out, 16)
            sp.wait_ge(y_out, 16)

        @block.gpsimd
        def _(pool):
            nc.gpsimd.iota(row_ids_i[:], pattern=[[1, CHUNKS]], base=0, channel_multiplier=CHUNKS).then_inc(row_ids_made, 1)
            nc.gpsimd.memset(ident[:], 0.0).then_inc(ident_zeroed, 1)
            pool.wait_ge(ident_zeroed, 1)
            nc.gpsimd.affine_select(out=ident[:], in_=ident[:], compare_op=ALU.not_equal, fill=1.0, base=0,
                                    pattern=[[-1, P]], channel_multiplier=1).then_inc(ident_ready, 1)
            pool.wait_ge(ids_in, 16)
            for t in range(TILES):
                for f in range(GATHERED):
                    k = max(k for k in range(QUADS) if QSTART[k] <= f)
                    if t >= 2 and f == QSTART[k]:
                        pool.wait_ge(turned, (t - 2) * QUADS + k + 1)
                    nc.gpsimd.indirect_dma_start(
                        out=rows[:, t % 2, f, :], out_offset=None, in_=tables[SLOTS[f]],
                        in_offset=bass.IndirectOffsetOnAxis(ap=ids_sb[:, t, f:f + 1], axis=0),
                    ).then_inc(rows_in[t % 2][k], 16)

        @block.tensor
        def _(pe):
            pe.wait_ge(ident_ready, 1)
            for _ in range(WARM_UP):
                nc.tensor.transpose(mlp_ps[:, 1, 0:P], ident[:], ident[:])
            pe.wait_ge(dense_in, 16)
            for t in range(TILES):
                last = nc.tensor.transpose(mlp_ps[:, 0, t * P:(t + 1) * P], dense_wide[:, t, :], ident[:])
            last.then_inc(dense_turned, 1)

            def sum_up(x, h, half, parts):
                for part in parts:
                    if half == 0 and part is table_lo:
                        pe.wait_ge(lo_ready, x + 1)
                    for c in range(HALF):
                        last = nc.tensor.matmul(gram_ps[:, h, 0, :], part[:, h, half * HALF + c, :], onehot[:, h, half, c, :],
                                                start=(half == 0 and c == 0 and part is table_hi),
                                                stop=(half == 1 and c == HALF - 1 and part is table_lo))
                return last

            def half_ready(x, half):
                pe.wait_ge(onehot_v, 2 * x + (half + 1))
                pe.wait_ge(onehot_s, 2 * x + (half + 1))

            def look_up(x, h, peeled):
                pe.wait_ge(hi_ready, x + 1)
                if not peeled:
                    pe.wait_ge(lookup_copied, x - 1)
                for half in range(2):
                    half_ready(x, half)
                    sum_up(x, h, half, (table_hi, table_lo)).then_inc(lookup_summed, 1)

            def turn(t, k):
                n = t * QUADS + k
                pe.wait_ge(rows_in[t % 2][k], (t // 2 + 1) * 16 * QCOUNT[k])
                if n >= 2:
                    pe.wait_ge(emb_odd if n % 2 else emb_even, n // 2)
                for m in range(QCOUNT[k]):
                    last = nc.tensor.transpose(turn_ps[:, n % 2, m, :], rows[:, t % 2, QSTART[k] + m, :], ident[:])
                last.then_inc(turned, 1)

            def gram(t):
                pe.wait_ge(emb_even, ((t + 1) * QUADS + 1) // 2)
                pe.wait_ge(emb_odd, (t + 1) * QUADS // 2)
                pe.wait_ge(mids_repeated, min(t + 1, 2))
                for u in range(UNITS):
                    n = t * UNITS + u
                    if n >= 2:
                        pe.wait_ge(unpacked_v, n - 1)
                        pe.wait_ge(unpacked_s, n - 1)
                    if n == 1:
                        pe.wait_ge(lookup_copied, ONEHOT + 1)
                    for m in range(UNIT):
                        r = u * UNIT + m
                        out = gram_ps[:, u % 2, m // PER_BANK, (m % PER_BANK) * BLOCK:(m % PER_BANK + 1) * BLOCK]
                        last = nc.tensor.matmul(out, emb[:, t, r, :, :].rearrange("d c f -> d (c f)"),
                                                emb[:, t, r, :, 0:FEATS], start=True, stop=True)
                    last.then_inc(gram_done, 1)

            def layer1(t, c):
                if c == (0 if t == TILES - 1 else 2):
                    pe.wait_ge(unpacked_v, (t + 1) * UNITS)
                    pe.wait_ge(unpacked_s, (t + 1) * UNITS)
                if c == 2 and 0 < t < TILES - 1:
                    pe.wait_ge(hid2_ready_s, t)
                    if t > 1:
                        pe.wait_ge(y_copied, t - 1)
                if c == 0 and t < TILES - 1:
                    pe.wait_ge(dense_copied, 1)
                    if t > 0:
                        pe.wait_ge(hid2_ready_v, t)
                if t == 0 and c == 2:
                    pe.wait_ge(weights_in, N_WEIGHTS)
                for q in range(JQ):
                    last = nc.tensor.matmul(hid1_sums(t, c), w1_sb[:, c, q, :], pairs[:, q, :],
                                            start=(q == 0), stop=(q == JQ - 1))
                if c % 2 == 1 or t == TILES - 1:
                    last.then_inc(hid1_summed, 1)

            def last_layers():
                t = TILES - 1
                layer1(t, 0)
                layer3(t - 1)
                for c in range(1, C1):
                    layer1(t, c)
                for k in range(C1):
                    pe.wait_ge(hid1_ready_v if k < 2 else hid1_ready_s, t + k % 2 + 1)
                    for c in (1, 0):
                        if c == 1 and k == 0:
                            pe.wait_ge(y_copied, t)
                        last = nc.tensor.matmul(hid2_ps[c], w2_cols[:, k, c, :], hid1[:, k, :],
                                                start=(k == 0), stop=(k == C1 - 1))
                        if k == C1 - 1:
                            last.then_inc(hid2_summed, 1)

            def layer2(t):
                pe.wait_ge(hid1_ready_v, t + 1)
                pe.wait_ge(hid1_ready_s, t + 1)
                for c in (1, 0):
                    if c == 1 and t > 0:
                        pe.wait_ge(y_copied, t)
                    for k in range(C1):
                        last = nc.tensor.matmul(hid2_ps[c], w2_cols[:, k, c, :], hid1[:, k, :],
                                                start=(k == 0), stop=(k == C1 - 1))
                    last.then_inc(hid2_summed, 1)

            def layer3(t):
                if t + 1 < TILES - 1:
                    pe.wait_ge(hid1_ready_s, t + 2)
                for ready, c in ((hid2_ready_s, 1), (hid2_ready_v, 0)):
                    pe.wait_ge(ready, t + 1)
                    last = nc.tensor.matmul(y_ps, w3_sb[:, c:c + 1], hid2[:, c, :], start=(c == 1), stop=(c == 0))
                last.then_inc(y_summed, 1)

            look_up(0, 0, True)
            look_up(1, 1, True)
            with pe.Fori(1, PAIRS - 1) as i:
                look_up(2 * i, 0, False)
                look_up(2 * i + 1, 1, False)
            x = ONEHOT - 2
            look_up(x, 0, False)
            turn(0, 0)
            turn(0, 1)
            x = ONEHOT - 1
            pe.wait_ge(hi_ready, x + 1)
            pe.wait_ge(lookup_copied, x - 1)
            half_ready(x, 0)
            sum_up(x, 1, 0, (table_hi, table_lo)).then_inc(lookup_summed, 1)
            turn(0, 2)
            turn(0, 3)
            half_ready(x, 1)
            sum_up(x, 1, 1, (table_hi,))
            for k in range(4, QUADS):
                turn(0, k)
            sum_up(x, 1, 1, (table_lo,)).then_inc(lookup_summed, 1)
            pe.wait_ge(lookup_copied, ONEHOT)
            for t in range(TILES):
                gram(t)
                if t > 0:
                    layer2(t - 1)
                if t + 1 < TILES:
                    turn(t + 1, 0)
                    turn(t + 1, 1)
                if t == TILES - 1:
                    last_layers()
                    break
                for n, c in enumerate((2, 3, 0, 1)):
                    layer1(t, c)
                    if t > 0 and c == 0:
                        layer3(t - 1)
                    if t + 1 < TILES and n < 3:
                        turn(t + 1, n + 2)
                    if t + 1 < TILES and n == (3 if t == TILES - 2 else 2):
                        turn(t + 1, QUADS - 1)
            layer3(TILES - 1)

        @block.vector
        def _(dve):
            nc.vector.memset(dense_wide[:], 0.0).then_inc(dense_zeroed, 1)
            nc.vector.memset(pairs[:], 0.0).then_inc(pairs_zeroed, 1)
            dve.wait_ge(row_ids_made, 1)
            nc.vector.tensor_copy(row_ids[:], row_ids_i[:]).then_inc(row_ids_ready, 1)
            dve.wait_ge(row_ids_ready, 1)

            def operands(x, h, peeled, very_first=False):
                ids_x = ids_wide[0:VP, bass.ds(x, 1), :].rearrange("p a b -> p (a b)")
                for half in range(2):
                    if not peeled:
                        dve.wait_ge(lookup_summed, 2 * x + (half - 3))
                    for c in range(HALF - 1):
                        row = half * HALF + c
                        last = nc.vector.tensor_scalar(onehot[:, h, half, c, :], ids_x, row_ids[:, row:row + 1], None, ALU.is_equal)
                    last.then_inc(onehot_v, 1)
                    if half == (1 if very_first else 0):
                        dve.wait_ge(hi_ready, x + 1)
                        nc.vector.tensor_tensor(table_lo[:, h], table[:, h], table_hi[:, h].bitcast(fp32),
                                                ALU.subtract).then_inc(lo_ready, 1)

            def quads(t, a, b):
                for k in range(a, b):
                    if (t * QUADS + k) % 2 == 0:
                        dve.wait_ge(turned, t * QUADS + k + 1)
                        copy_quad(nc.vector.tensor_copy, t, k).then_inc(emb_even, 1)

            def relu2(t):
                dve.wait_ge(hid2_summed, C2 * (t + 1))
                nc.vector.tensor_scalar(hid2[:, 0, :], hid2_ps[0], b2_sb[:, 0:1], 0.0,
                                        ALU.add, ALU.max).then_inc(hid2_ready_v, 1)

            dve.wait_ge(ids_wide_in[0], 16)
            operands(0, 0, True, very_first=True)
            dve.wait_ge(ids_wide_in[1], 16)
            operands(1, 1, True)
            with dve.Fori(1, PAIRS) as i:
                dve.wait_ge(ids_pairs_in, 16 * i)
                operands(2 * i, 0, False)
                operands(2 * i + 1, 1, False)
            dve.wait_ge(dense_turned, 1)
            nc.vector.tensor_copy(dense_t[DENSE_P:, :], mlp_ps[DENSE_P:, 0, :]).then_inc(dense_copied, 1)
            quads(0, 0, QUADS - 1)
            dve.wait_ge(lookup_copied, LAST - GATHERED)
            repeat_mids(nc.vector.tensor_copy, slice(0, 1)).then_inc(mids_repeated, 1)
            quads(0, QUADS - 1, QUADS)
            repeat_mids(nc.vector.tensor_copy, slice(1, TILES)).then_inc(mids_repeated, 1)
            dve.wait_ge(weights_in, N_WEIGHTS)
            dve.wait_ge(pairs_zeroed, 1)
            for t in range(TILES):
                for u in range(UNITS):
                    dve.wait_ge(gram_done, t * UNITS + u + 1)
                    unpack_unit(dve, nc.vector.tensor_copy, t, u, (0, 1), under_v, apart_v).then_inc(unpacked_v, 1)
                if t > 0:
                    relu2(t - 1)
                if t + 1 < TILES:
                    quads(t + 1, 0, QUADS)
                dve.wait_ge(hid1_summed, 2 * t + (1 if t == TILES - 1 else 2))
                for c in (0, 1):
                    if t == TILES - 1 and c == 1:
                        last.then_inc(hid1_ready_v, 1)
                        dve.wait_ge(hid1_summed, 2 * t + 2)
                    last = nc.vector.tensor_scalar(hid1[:, c, :], hid1_sums(t, c), b1_sb[:, c:c + 1], 0.0, ALU.add, ALU.max)
                last.then_inc(hid1_ready_v, 1)
            relu2(TILES - 1)

        @block.scalar
        def _(act):
            act.wait_ge(row_ids_made, 1)
            nc.scalar.activation(minus_row_ids[:], row_ids_i[:], ACT.Copy, scale=-1.0).then_inc(minus_row_ids_ready, 1)
            act.wait_ge(minus_row_ids_ready, 1)
            act.wait_ge(ids_wide_in[0], 16)

            def take_high(x, h, loads, peeled):
                act.wait_ge(table_in[h], 32 * loads)
                if not peeled:
                    act.wait_ge(lookup_summed, 2 * x - 2)
                nc.scalar.copy(table_hi[:, h], table[:, h]).then_inc(hi_ready, 1)

            def take_distance(x, n, half):
                row = half * HALF + HALF - 1
                nc.scalar.activation(distance[:, half, 0:n, :], ids_wide[0:VP, bass.ds(x, n), :], ACT.Abs,
                                     bias=minus_row_ids[:, row:row + 1]).then_inc(distance_ready, 1)

            def take_onehot(h, half, distances):
                act.wait_ge(distance_ready, distances)
                nc.scalar.activation(onehot[:, h, half, HALF - 1, :], distance[:, half, h, :], ACT.Relu,
                                     bias=1.0, scale=-1.0).then_inc(onehot_s, 1)

            def copy_sums(x, h, tiles=slice(0, TILES)):
                act.wait_ge(lookup_summed, 2 * x + 2)
                slot = emb[:, tiles, :, :, bass.ds(GATHERED + x, 1)].rearrange("d t r c f -> d t c (r f)")
                sums = gram_ps[:, h, 0, :].rearrange("d (t c r) -> d t c r", t=TILES, c=CLASSES)
                nc.scalar.copy(slot, sums[:, tiles]).then_inc(lookup_copied, 1)

            def quads(t, a, b):
                for k in range(a, b):
                    if (t * QUADS + k) % 2 == 1:
                        act.wait_ge(turned, t * QUADS + k + 1)
                        copy_quad(nc.scalar.copy, t, k).then_inc(emb_odd, 1)

            def relu2(t):
                act.wait_ge(hid2_summed, C2 * t + 1)
                nc.scalar.activation(hid2[:, 1, :], hid2_ps[1], ACT.Relu, bias=b2_sb[:, 1:2]).then_inc(hid2_ready_s, 1)

            def copy_y(t):
                act.wait_ge(y_summed, t + 1)
                nc.scalar.copy(y_sb[:, t * P:(t + 1) * P], y_ps).then_inc(y_copied, 1)

            take_distance(0, 1, 0)
            take_onehot(0, 0, 1)
            take_high(0, 0, 1, True)
            take_distance(0, 1, 1)
            take_onehot(0, 1, 2)
            act.wait_ge(ids_wide_in[1], 16)
            take_high(1, 1, 1, True)
            for half in range(2):
                row = half * HALF + HALF - 1
                nc.scalar.activation(distance[:, half, 1, :], ids_wide[0:VP, 1, :], ACT.Abs,
                                     bias=minus_row_ids[:, row:row + 1]).then_inc(distance_ready, 1)
            take_onehot(1, 0, 3)
            take_onehot(1, 1, 4)
            act.wait_ge(ids_pairs_in, 16)
            act.wait_ge(onehot_s, 3)
            take_distance(2, 2, 0)

            def pair(i, last):
                x = 2 * i
                act.wait_ge(onehot_s, 2 * x)
                take_high(x, 0, i + 1, False)
                take_onehot(0, 0, 2 * i + 3)
                copy_sums(x - 2, 0)
                take_distance(x, 2, 1)
                take_onehot(0, 1, 2 * i + 4)
                take_high(x + 1, 1, i + 1, False)
                take_onehot(1, 0, 2 * i + 3)
                copy_sums(x - 1, 1)
                if not last:
                    act.wait_ge(onehot_s, 2 * x + 3)
                    act.wait_ge(ids_pairs_in, 16 * i + 16)
                take_onehot(1, 1, 2 * i + 4)
                if not last:
                    take_distance(x + 2, 2, 0)

            with act.Fori(1, PAIRS - 1) as i:
                pair(i, False)
            pair(PAIRS - 1, True)
            copy_sums(ONEHOT - 2, 0)
            quads(0, 0, QUADS)
            copy_sums(ONEHOT - 1, 1, slice(0, 1))
            copy_sums(ONEHOT - 1, 1, slice(1, TILES))
            act.wait_ge(weights_in, N_WEIGHTS)
            act.wait_ge(pairs_zeroed, 1)
            act.wait_ge(dense_copied, 1)
            for t in range(TILES):
                for u in range(UNITS):
                    act.wait_ge(gram_done, t * UNITS + u + 1)
                    last = unpack_unit(act, nc.scalar.copy, t, u, (2, 3), under_s, apart_s)
                    if u == UNITS - 1:
                        act.wait_ge(apart_v, (t + 1) * UNITS)
                        last = nc.scalar.copy(pairs[DENSE_P:DENSE_P + DENSE, JQ - 1, :],
                                              dense_t[DENSE_P:DENSE_P + DENSE, t * P:(t + 1) * P])
                    last.then_inc(unpacked_s, 1)
                if t > 0:
                    relu2(t - 1)
                if t + 1 < TILES:
                    quads(t + 1, 0, 3)
                if t == TILES - 1:
                    copy_y(t - 1)
                act.wait_ge(hid1_summed, 2 * t + (3 if t == TILES - 1 else 1))
                for c in (2, 3):
                    if t == TILES - 1 and c == 3:
                        last.then_inc(hid1_ready_s, 1)
                        act.wait_ge(hid1_summed, 2 * t + 4)
                    last = nc.scalar.activation(hid1[:, c, :], hid1_sums(t, c), ACT.Relu, bias=b1_sb[:, c:c + 1])
                last.then_inc(hid1_ready_s, 1)
                if t + 1 < TILES:
                    quads(t + 1, 3, QUADS)
                if 0 < t < TILES - 1:
                    copy_y(t - 1)
            relu2(TILES - 1)
            copy_y(TILES - 1)


def kernel(**inputs):
    import numpy as np
    import concourse.bacc as bacc
    from concourse.bass_utils import run_bass_kernel_spmd

    arrays = {name: np.ascontiguousarray(value) for name, value in inputs.items()}
    w1 = arrays["W_top1"]
    laid = np.zeros((P, JQ, H1), w1.dtype)
    for a in range(FEATS):
        for b in range(a + 1, FEATS):
            if a < SHORT and b == LAST:
                head, row = HEADS - 2, a
            elif a < HEADS:
                head, row = a, b
            elif b < LAST:
                head, row = a - HEADS, b + FEATS - COPIED
            else:
                head, row = a - HEADS, LAST
            lo, hi = sorted((SLOTS[a], SLOTS[b]))
            laid[SLOT * (head // JQ) + row, head % JQ] = w1[hi * (hi - 1) // 2 + lo]
    laid[DENSE_P:DENSE_P + DENSE, JQ - 1] = w1[FEATS * (FEATS - 1) // 2:]
    arrays["W_top1"] = np.ascontiguousarray(laid.reshape(P, JQ, P, C1).transpose(0, 3, 1, 2))
    arrays["ids_t"] = np.ascontiguousarray(arrays["ids"].T[SLOTS[GATHERED:]])
    arrays["ids"] = np.ascontiguousarray(arrays["ids"][:, SLOTS[:GATHERED]])

    nc = bacc.Bacc("TRN2", target_bir_lowering=False, num_devices=1)
    aps = {name: nc.dram_tensor(f"in_{name}", a.shape, mybir.dt.from_np(a.dtype), kind="ExternalInput").ap()
           for name, a in arrays.items()}
    y = nc.dram_tensor("y", (BATCH, 1), mybir.dt.float32, kind="ExternalOutput").ap()
    program(nc, aps["ids"], aps["ids_t"], [aps[f"tbl_{f}"] for f in range(FEATS)], aps["dense_ctx"],
            aps["W_top1"], aps["b_top1"], aps["W_top2"], aps["b_top2"], aps["W_top3"], y)
    got = run_bass_kernel_spmd(nc, [{f"in_{name}": a for name, a in arrays.items()}], core_ids=[0])
    return got.results[0]["y"]
```
